# Optimizing a Trainium2 kernel written in Bass

```python
import numpy as np
import jax
import jax.numpy as jnp

def _softmax(x, axis=-1):
    return jax.nn.softmax(x, axis=axis)

def _gelu(x):
    return jax.nn.gelu(x, approximate=True)

def _silu(x):
    return jax.nn.silu(x)

def _sigmoid(x):
    return jax.nn.sigmoid(x)

def _layernorm(x, axis=-1, eps=1e-05):
    m = jnp.mean(x, axis=axis, keepdims=True)
    v = jnp.var(x, axis=axis, keepdims=True)
    return (x - m) / jnp.sqrt(v + eps)

def _scatter_add(tgt, idx, src, axis=0):
    return tgt.at[idx].add(src)

def _segment_sum(src, seg, n):
    return jax.ops.segment_sum(src, seg, n)
kernel_name = 'mk_rec_standalone_d1_rec_r8_f1ada3'

def setup_inputs(seed: int=0):
    np.random.seed(seed)
    _w = jnp.asarray

    def _rec_inputs():
        import jax
        import jax.numpy as jnp
        _rk = jax.random.key(seed)
        r_x0 = jax.random.randint(jax.random.fold_in(_rk, 1), (512, 12500), 0, 2, jnp.int32)
        return r_x0
    r_x0 = _rec_inputs()

    def _L0_rec_setup():
        import jax, jax.numpy as jnp
        import numpy as np
        FIELD_DIMS = 12500
        FACTORS = 16
        BATCH = 1024
        key = jax.random.key(seed)
        k1, k2 = jax.random.split(key)
        x0 = jax.random.randint(k1, (BATCH, FIELD_DIMS), 0, 2, dtype=jnp.int32)
        W = jax.random.normal(k2, (FIELD_DIMS, FACTORS), dtype=jnp.float32) * 0.05
        return {'x0': x0, 'W': W}
    _L0_rec_all = _L0_rec_setup()
    _L0_rec_in = {k: v for k, v in _L0_rec_all.items() if k in ('W',)}
    del _L0_rec_all
    return {'r_x0': r_x0, 'L0_rec_W': _L0_rec_in['W']}

def reference(r_x0, L0_rec_W):
    import jax
    import jax.numpy as jnp

    def _L0_rec_ref(x0, W):
        import jax, jax.numpy as jnp
        import numpy as np
        FIELD_DIMS = 12500
        FACTORS = 16
        BATCH = 1024
        m = (x0 > 0).astype(W.dtype)
        s = m @ W
        q = m @ jnp.sum(W * W, axis=-1)
        return 0.5 * (jnp.sum(s * s, axis=-1) - q)
    y = _L0_rec_ref(r_x0, L0_rec_W)
    return y

_drawn_inputs = setup_inputs


def setup_inputs(seed=0):
    import zlib

    import numpy as np

    out = dict(_drawn_inputs(seed))
    spreads = {}
    factors = {}
    for name, (base, spread) in spreads.items():
        noise = np.random.default_rng([zlib.crc32(name.encode()), seed]).standard_normal(out[name].shape)
        drawn = base * np.exp(spread * noise) if base else spread * noise
        out[name] = jnp.asarray(drawn.astype(out[name].dtype))
    for name, factor in factors.items():
        out[name] = (out[name] * factor).astype(out[name].dtype)
    return out
```

```python
from contextlib import ExitStack

import concourse.bass as bass
from concourse import mybir
from concourse.alu_op_type import AluOpType as ALU

F32 = mybir.dt.float32
BF16 = mybir.dt.bfloat16
I32 = mybir.dt.int32
AX_X = mybir.AxisListType.X

P = 128
PARTS = 3
SLOTS = 4
CHUNK = 7
TAIL = (6, 4, 2, 1)


def plan(fields):
    full = fields // P
    short = fields - full * P
    turn = SLOTS * CHUNK
    turns = (full - sum(TAIL)) // turn
    assert short > 0 and turns * turn + sum(TAIL) == full
    return full, short, turns


def fm_pairwise_kernel(nc: bass.Bass, x_full: bass.AP, x_short: bass.AP, w_full: bass.AP, w_short: bass.AP,
                       y: bass.AP):
    batch = x_full.shape[1]
    factors = w_short.shape[1]
    full, short, turns = plan(x_full.shape[0] + x_short.shape[0])
    groups = batch // P
    cols = factors + 1
    tiles = full + 1
    turn_tiles = SLOTS * CHUNK
    tail_start = [turns * turn_tiles + sum(TAIL[:j]) for j in range(len(TAIL))]

    def x_rows(first_tile, n):
        return x_full[bass.ds(first_tile * P, n * P), :].rearrange("(p t) b -> p (t b)", t=n)

    with ExitStack() as ctx:
        def sb(name, shape, dt):
            return ctx.enter_context(nc.sbuf_tensor(name, shape, dt))

        def sem(name):
            return ctx.enter_context(nc.semaphore(name))

        x_head = sb("x_head", [P, batch], I32)
        m_head = sb("m_head", [P, batch], BF16)
        x_ring = [sb(f"x_ring{s}", [P, CHUNK * batch], I32) for s in range(SLOTS)]
        m_ring = [sb(f"m_ring{s}", [P, CHUNK, batch], BF16) for s in range(SLOTS)]
        x_tail = [sb(f"x_tail{j}", [P, n * batch], I32) for j, n in enumerate(TAIL)]
        m_tail = [sb(f"m_tail{j}", [P, n, batch], BF16) for j, n in enumerate(TAIL)]

        w = sb("w", [P, tiles * factors], F32)
        w_parts = sb("w_parts", [P, tiles * PARTS * cols], BF16)
        w_by_tile = w[:, :].rearrange("p (t f) -> p t f", f=factors)
        w_parts_by_tile = w_parts[:, :].rearrange("p (t k c) -> p t k c", k=PARTS, c=cols)
        square = sb("square", [P, tiles, factors], F32)
        wide = sb("wide", [P, tiles, cols], F32)

        sums = sb("sums", [P, groups, cols], F32)
        y_sb = sb("y_sb", [P, groups], F32)
        acc = ctx.enter_context(nc.psum_tensor("acc", [P, groups, 512], F32))

        w_cleared = sem("w_cleared")
        w_full_landed = sem("w_full_landed")
        w_short_landed = sem("w_short_landed")
        wide_copied = sem("wide_copied")
        squared = sem("squared")
        wide_summed = sem("wide_summed")
        part_0_done = sem("part_0_done")
        rest_done = sem("rest_done")
        part_1_done = sem("part_1_done")
        w_ready = sem("w_ready")
        head_landed = sem("head_landed")
        head_masked = sem("head_masked")
        ring_landed = [sem(f"ring_landed{s}") for s in range(SLOTS)]
        ring_masked = [sem(f"ring_masked{s}") for s in range(SLOTS)]
        ring_multiplied = [sem(f"ring_multiplied{s}") for s in range(SLOTS)]
        tail_landed = [sem(f"tail_landed{j}") for j in range(len(TAIL))]
        tail_masked = [sem(f"tail_masked{j}") for j in range(len(TAIL))]
        acc_done = sem("acc_done")
        finish_step = sem("finish_step")
        y_written = sem("y_written")

        block = ctx.enter_context(nc.Block())

        @block.sync
        def _(sp):
            sp.dma_start(w[:, factors:], w_full[:, :]).then_inc(w_full_landed, 16)
            sp.dma_start(x_head[0:short, :], x_short[:, :]).then_inc(head_landed, 16)
            sp.wait_ge(w_cleared, 1)
            sp.dma_start(w[0:short, 0:factors], w_short[:, :]).then_inc(w_short_landed, 16)
            for s in range(SLOTS):
                sp.dma_start(x_ring[s][:, :], x_rows(s * CHUNK, CHUNK)).then_inc(ring_landed[s], 16)
            with sp.Fori(1, turns) as turn:
                for s in range(SLOTS):
                    sp.wait_ge(ring_masked[s], turn)
                    sp.dma_start(x_ring[s][:, :], x_rows(turn * turn_tiles + s * CHUNK, CHUNK)).then_inc(
                        ring_landed[s], 16)
            for j, n in enumerate(TAIL):
                sp.dma_start(x_tail[j][:, :], x_rows(tail_start[j], n)).then_inc(tail_landed[j], 16)
            sp.wait_ge(finish_step, 3)
            sp.dma_start(y[:, :], y_sb[:, :]).then_inc(y_written, 16)
            sp.wait_ge(y_written, 16)

        @block.scalar
        def _(act):
            act.wait_ge(w_full_landed, 16)
            act.wait_ge(w_short_landed, 16)
            nc.scalar.copy(wide[:, :, 0:factors], w_by_tile).then_inc(wide_copied, 1)
            act.wait_ge(wide_copied, 1)
            act.wait_ge(wide_summed, 1)
            nc.scalar.copy(w_parts_by_tile[:, :, 0, :], wide[:, :, :]).then_inc(part_0_done, 1)
            act.wait_ge(rest_done, 1)
            nc.scalar.copy(w_parts_by_tile[:, :, 1, :], wide[:, :, :]).then_inc(part_1_done, 1)

        def mask(out, x):
            return nc.vector.tensor_scalar(out, x, 0.0, None, ALU.is_gt)

        @block.vector
        def _(dve):
            nc.vector.memset(w[:, 0:factors], 0.0).then_inc(w_cleared, 1)
            dve.wait_ge(w_full_landed, 16)
            dve.wait_ge(w_short_landed, 16)
            nc.vector.scalar_tensor_tensor(out=square[:, :, :], in0=w_by_tile, scalar=-0.5, in1=w_by_tile,
                                           op0=ALU.mult, op1=ALU.mult).then_inc(squared, 1)
            dve.wait_ge(squared, 1)
            nc.vector.tensor_reduce(wide[:, :, factors:cols], square[:, :, :], AX_X, ALU.add).then_inc(wide_summed, 1)
            dve.wait_ge(head_landed, 16)
            mask(m_head[0:short, :], x_head[0:short, :]).then_inc(head_masked, 1)
            dve.wait_ge(part_0_done, 1)
            nc.vector.tensor_tensor(wide[:, :, :], wide[:, :, :], w_parts_by_tile[:, :, 0, :],
                                    ALU.subtract).then_inc(rest_done, 1)
            dve.wait_ge(part_1_done, 1)
            nc.vector.tensor_tensor(w_parts_by_tile[:, :, 2, :], wide[:, :, :], w_parts_by_tile[:, :, 1, :],
                                    ALU.subtract).then_inc(w_ready, 1)

            for s in range(SLOTS):
                dve.wait_ge(ring_landed[s], 16)
                mask(m_ring[s][:, :, :].rearrange("p t b -> p (t b)"), x_ring[s][:, :]).then_inc(ring_masked[s], 1)
            with dve.Fori(1, turns) as turn:
                for s in range(SLOTS):
                    dve.wait_ge(ring_landed[s], 16 * turn + 16)
                    dve.wait_ge(ring_multiplied[s], turn)
                    mask(m_ring[s][:, :, :].rearrange("p t b -> p (t b)"), x_ring[s][:, :]).then_inc(
                        ring_masked[s], 1)
            for j in range(len(TAIL)):
                dve.wait_ge(tail_landed[j], 16)
                mask(m_tail[j][:, :, :].rearrange("p t b -> p (t b)"), x_tail[j][:, :]).then_inc(tail_masked[j], 1)

            dve.wait_ge(acc_done, 1)
            nc.vector.tensor_reduce(sums[:, :, :],
                                    acc[:, :, 0:PARTS * cols].rearrange("p g (k c) -> p g c k", k=PARTS),
                                    AX_X, ALU.add).then_inc(finish_step, 1)
            dve.wait_ge(finish_step, 1)
            nc.vector.scalar_tensor_tensor(out=sums[:, :, 0:factors], in0=sums[:, :, 0:factors], scalar=0.5,
                                           in1=sums[:, :, 0:factors], op0=ALU.mult,
                                           op1=ALU.mult).then_inc(finish_step, 1)
            dve.wait_ge(finish_step, 2)
            nc.vector.tensor_reduce(y_sb[:, :], sums[:, :, :], AX_X, ALU.add).then_inc(finish_step, 1)

        @block.tensor
        def _(pe):
            def multiply(m, tile, first=False, last=False):
                k = m.shape[0]
                for g in range(groups):
                    product = nc.tensor.matmul(acc[:, g, 0:PARTS * cols], m[:, g * P:(g + 1) * P],
                                               w_parts[0:k, bass.ds(tile * (PARTS * cols), PARTS * cols)],
                                               start=first, stop=last)
                return product

            pe.wait_ge(w_ready, 1)
            pe.wait_ge(head_masked, 1)
            multiply(m_head[0:short, :], 0, first=True)
            with pe.Fori(0, turns) as turn:
                for s in range(SLOTS):
                    pe.wait_ge(ring_masked[s], turn + 1)
                    for t in range(CHUNK):
                        product = multiply(m_ring[s][:, t, :], 1 + turn * turn_tiles + s * CHUNK + t)
                    product.then_inc(ring_multiplied[s], 1)
            for j, n in enumerate(TAIL):
                pe.wait_ge(tail_masked[j], 1)
                for t in range(n):
                    product = multiply(m_tail[j][:, t, :], 1 + tail_start[j] + t,
                                       last=(j == len(TAIL) - 1 and t == n - 1))
            product.then_inc(acc_done, 1)


def kernel(r_x0, L0_rec_W):
    import numpy as np
    import concourse.bacc as bacc
    from concourse.bass_utils import run_bass_kernel_spmd

    x = np.asarray(r_x0)
    weights = np.asarray(L0_rec_W)
    batch, fields = x.shape
    factors = weights.shape[1]
    groups = batch // P
    full, short, turns = plan(fields)

    x_t = np.ascontiguousarray(x.reshape(P, groups, fields).transpose(2, 1, 0)).reshape(fields, batch)
    chunks = [CHUNK] * (turns * SLOTS) + list(TAIL)
    w_chunks, at = [], 0
    for n in chunks:
        w_chunks.append(weights[at:at + n * P].reshape(P, n * factors))
        at += n * P
    arrays = {
        "x_full": x_t[:full * P],
        "x_short": x_t[full * P:],
        "w_full": np.concatenate(w_chunks, axis=1),
        "w_short": np.ascontiguousarray(weights[full * P:]),
    }

    nc = bacc.Bacc("TRN2", target_bir_lowering=False, num_devices=1)
    args = [nc.dram_tensor(name, a.shape, mybir.dt.from_np(a.dtype), kind="ExternalInput").ap()
            for name, a in arrays.items()]
    args.append(nc.dram_tensor("y", (P, groups), F32, kind="ExternalOutput").ap())
    fm_pairwise_kernel(nc, *args)
    result = run_bass_kernel_spmd(nc, [arrays], core_ids=[0])
    return result.results[0]["y"].reshape(batch)
```
